# Optimizing a Trainium2 kernel written in Bass

```python
import numpy as np
import jax
import jax.numpy as jnp

def _softmax(x, axis=-1):
    return jax.nn.softmax(x, axis=axis)

def _gelu(x):
    return jax.nn.gelu(x, approximate=True)

def _silu(x):
    return jax.nn.silu(x)

def _sigmoid(x):
    return jax.nn.sigmoid(x)

def _layernorm(x, axis=-1, eps=1e-05):
    m = jnp.mean(x, axis=axis, keepdims=True)
    v = jnp.var(x, axis=axis, keepdims=True)
    return (x - m) / jnp.sqrt(v + eps)

def _scatter_add(tgt, idx, src, axis=0):
    return tgt.at[idx].add(src)

def _segment_sum(src, seg, n):
    return jax.ops.segment_sum(src, seg, n)
kernel_name = 'mk_adj_resnorm_d1_adj_r2_9d6381'

def setup_inputs(seed: int=0):
    np.random.seed(seed)
    _w = jnp.asarray

    def _rec_inputs():
        import jax
        import jax.numpy as jnp
        _gk = jax.random.key(seed)
        x = -0.0005207 + 1.001 * jax.random.normal(jax.random.fold_in(_gk, 1), (4096, 128), jnp.float32)
        _w = (1.0 + jnp.arange(4096, dtype=jnp.float32)) ** (-0.5)
        _w = _w / _w.mean()
        _pij = jnp.clip(0.000488281 * _w[:, None] * _w[None, :], 0.0, 1.0)
        _a = jax.random.uniform(jax.random.fold_in(_gk, 2), (4096, 4096)) < _pij
        _a = jnp.logical_or(_a, jnp.eye(4096, dtype=bool))
        _af = _a.astype(jnp.float32)
        _af = _af * jax.random.uniform(jax.random.fold_in(_gk, 3), (4096, 4096), jnp.float32, 0.05, 1)
        adj = _af
        return (x, adj)
    x, adj = _rec_inputs()

    def _L0_gnn_setup():
        import jax, jax.numpy as jnp
        import numpy as np
        N = 4096
        D = 128
        L = 3

        def _cxin_conv(x, a, eps, W, b):
            ax = a @ x
            h = ax + (1.0 + eps[0]) * ax
            for i in range(L):
                h = jax.nn.relu(h @ W[i].T + b[i])
            return h
        key = jax.random.key(seed)
        ks = jax.random.split(key, 8)
        s = 1.0 / np.sqrt(D)
        return {'x1': jax.random.normal(ks[0], (N, D), jnp.float32), 'x2': jax.random.normal(ks[1], (N, D), jnp.float32), 'G1': jax.random.uniform(ks[2], (N, N), jnp.float32), 'G2': jax.random.uniform(ks[3], (N, N), jnp.float32), 'eps1': jnp.zeros((1,), jnp.float32), 'eps2': jnp.zeros((1,), jnp.float32), 'W1': jax.random.normal(ks[4], (L, D, D), jnp.float32) * s, 'b1': jnp.zeros((L, D), jnp.float32), 'W2': jax.random.normal(ks[5], (L, D, D), jnp.float32) * s, 'b2': jnp.zeros((L, D), jnp.float32), 'Wm': jax.random.normal(ks[6], (D, 2 * D), jnp.float32) * (1.0 / np.sqrt(2 * D)), 'bm': jnp.zeros((D,), jnp.float32)}
    _L0_gnn_all = _L0_gnn_setup()
    _L0_gnn_in = {k: v for k, v in _L0_gnn_all.items() if k in ('x2', 'eps1', 'eps2', 'W1', 'b1', 'W2', 'b2', 'Wm', 'bm')}
    del _L0_gnn_all
    return {'x': x, 'adj': adj, 'L0_gnn_x2': _L0_gnn_in['x2'], 'L0_gnn_eps1': _L0_gnn_in['eps1'], 'L0_gnn_eps2': _L0_gnn_in['eps2'], 'L0_gnn_W1': _L0_gnn_in['W1'], 'L0_gnn_b1': _L0_gnn_in['b1'], 'L0_gnn_W2': _L0_gnn_in['W2'], 'L0_gnn_b2': _L0_gnn_in['b2'], 'L0_gnn_Wm': _L0_gnn_in['Wm'], 'L0_gnn_bm': _L0_gnn_in['bm']}

def reference(x, adj, L0_gnn_x2, L0_gnn_eps1, L0_gnn_eps2, L0_gnn_W1, L0_gnn_b1, L0_gnn_W2, L0_gnn_b2, L0_gnn_Wm, L0_gnn_bm):
    import jax
    import jax.numpy as jnp

    def _L0_gnn_ref(x1, x2, G1, G2, eps1, eps2, W1, b1, W2, b2, Wm, bm):
        import jax, jax.numpy as jnp
        import numpy as np
        N = 4096
        D = 128
        L = 3

        def _cxin_conv(x, a, eps, W, b):
            ax = a @ x
            h = ax + (1.0 + eps[0]) * ax
            for i in range(L):
                h = jax.nn.relu(h @ W[i].T + b[i])
            return h
        out1 = _cxin_conv(x1, G1, eps1, W1, b1)
        out2 = _cxin_conv(x2, G2, eps2, W2, b2)
        merged = jnp.concatenate((out1, out2), axis=1)
        return merged @ Wm.T + bm
    x = _layernorm(x + _L0_gnn_ref(x, L0_gnn_x2, adj, adj, L0_gnn_eps1, L0_gnn_eps2, L0_gnn_W1, L0_gnn_b1, L0_gnn_W2, L0_gnn_b2, L0_gnn_Wm, L0_gnn_bm), axis=-1)
    return x

_drawn_inputs = setup_inputs


def setup_inputs(seed=0):
    import zlib

    import numpy as np

    out = dict(_drawn_inputs(seed))
    spreads = {'L0_gnn_b1': (0.0, 0.1), 'L0_gnn_b2': (0.0, 0.1), 'L0_gnn_bm': (0.0, 0.1)}
    factors = {}
    for name, (base, spread) in spreads.items():
        noise = np.random.default_rng([zlib.crc32(name.encode()), seed]).standard_normal(out[name].shape)
        drawn = base * np.exp(spread * noise) if base else spread * noise
        out[name] = jnp.asarray(drawn.astype(out[name].dtype))
    for name, factor in factors.items():
        out[name] = (out[name] * factor).astype(out[name].dtype)
    return out
```

```python
from contextlib import ExitStack

import concourse.bass as bass
from concourse import mybir

ALU = mybir.AluOpType
ACT = mybir.ActivationFunctionType
F32 = mybir.dt.float32
F32R = mybir.dt.float32r

P = 128
N = 4096
D = 128
LAYERS = 3
T = N // P
COLS = 512
CHUNKS = N // COLS
TILES = COLS // P
GSLOTS = 2
GROUPS = T // GSLOTS
GCOLS = GSLOTS * COLS
RING = 8
LOADS = 4
LAG = 3
STEPS = GROUPS + LAG
XSLOTS = 4
XPIECES = T // XSLOTS
XCOLS = XSLOTS * D
XPG = XSLOTS // GSLOTS
EPS = 1e-5
NW = 2 * LAYERS + 2


def build(nc, x1, x2, adj, wts, bias, eps, bm, out):
    with ExitStack() as ctx:
        def sb(name, shape, dt=F32):
            return ctx.enter_context(nc.sbuf_tensor(name, shape, dt))

        def pb(name, shape):
            return ctx.enter_context(nc.psum_tensor(name, shape, F32))

        def sem(name):
            return ctx.enter_context(nc.semaphore(name))

        x1_sb = sb("x1_sb", [P, T * D])
        x2_in = sb("x2_in", [P, 2, XCOLS])
        x_hi = sb("x_hi", [P, 2, T * D], F32R)
        x_lo = sb("x_lo", [P, 2, T * D], F32R)
        a_in = sb("a_in", [P, LOADS, GCOLS])
        a_hi = sb("a_hi", [P, RING, GCOLS], F32R)
        a_lo = sb("a_lo", [P, RING, GCOLS], F32R)
        w_in = sb("w_in", [P, NW, D])
        w_hi = sb("w_hi", [P, NW, D], F32R)
        w_lo = sb("w_lo", [P, NW, D], F32R)
        bias_sb = sb("bias_sb", [P, 2 * LAYERS])
        eps_sb = sb("eps_sb", [P, 2])
        gain = sb("gain", [P, 2])
        bm_sb = sb("bm_sb", [P, D])
        ln_eps = sb("ln_eps", [P, 1])
        h = sb("h", [P, 2, COLS])
        h_hi = sb("h_hi", [P, 2, COLS], F32R)
        h_lo = sb("h_lo", [P, 2, COLS], F32R)
        y = sb("y", [P, COLS])
        stats = sb("stats", [P, TILES, 6])
        mv = sb("mv", [P, TILES, 2])
        std = sb("std", [P, TILES])
        rstd = sb("rstd", [P, TILES])
        normed = sb("normed", [P, COLS])

        acc = [pb(f"acc{b}", [P, COLS]) for b in range(2)]
        mlp = [pb(f"mlp{b}", [P, COLS]) for b in range(2)]
        merged = pb("merged", [P, COLS])

        a_loaded = [sem(f"a_loaded{s}") for s in range(LOADS)]
        x_loaded = [sem(f"x_loaded{s}") for s in range(2)]
        w_loaded = sem("w_loaded")
        small_loaded = sem("small_loaded")
        bm_loaded = sem("bm_loaded")
        a_hi_ready = sem("a_hi_ready")
        a_lo_ready = sem("a_lo_ready")
        group_used = sem("group_used")
        x_hi_ready = sem("x_hi_ready")
        x_lo_ready = sem("x_lo_ready")
        w_hi_ready = sem("w_hi_ready")
        w_lo_ready = sem("w_lo_ready")
        gain_ready = sem("gain_ready")
        ln_eps_ready = sem("ln_eps_ready")
        residual_ready = sem("residual_ready")
        acc1_done = sem("acc1_done")
        layer_done = [sem(f"layer_done{b}") for b in range(2)]
        h_ready = [sem(f"h_ready{b}") for b in range(2)]
        h_hi_ready = [sem(f"h_hi_ready{b}") for b in range(2)]
        h_lo_ready = [sem(f"h_lo_ready{b}") for b in range(2)]
        merge_done = sem("merge_done")
        y_ready = sem("y_ready")
        stats_ready = sem("stats_ready")
        var_ready = sem("var_ready")
        std_ready = sem("std_ready")
        rstd_ready = sem("rstd_ready")
        norm_ready = sem("norm_ready")
        stored = sem("stored")

        adj_rows = adj.rearrange("c g p n -> (c g p) n")
        x1_pieces = x1.rearrange("(p j t) d -> j p (t d)", p=P, j=XPIECES)
        x2_pieces = x2.rearrange("(p j t) d -> j p (t d)", p=P, j=XPIECES)
        out_chunks = out.rearrange("(p c t) d -> p c (t d)", p=P, c=CHUNKS)

        block = ctx.enter_context(nc.Block())

        @block.sync
        def _(sp):
            def load_group(c, g):
                if isinstance(c, int) and c == 0:
                    if g >= LOADS:
                        sp.wait_ge(a_lo_ready, g - LOADS + 1)
                else:
                    sp.wait_ge(a_lo_ready, c * GROUPS + (g - LOADS + 1))
                sp.dma_start(a_in[:, g % LOADS, :],
                             adj_rows[bass.ds((c * GROUPS + g) * P, P), :]).then_inc(a_loaded[g % LOADS], 16)

            def load_x(j):
                if j >= 2:
                    sp.wait_ge(x_lo_ready, 2 * (j - 1))
                sp.dma_start(x1_sb[:, j * XCOLS:(j + 1) * XCOLS], x1_pieces[j]).then_inc(x_loaded[j % 2], 16)
                sp.dma_start(x2_in[:, j % 2, :], x2_pieces[j]).then_inc(x_loaded[j % 2], 16)

            load_x(0)
            load_group(0, 0)
            load_group(0, 1)
            load_x(1)
            for g in range(2, GROUPS):
                load_group(0, g)
                if g % XPG == 1 and g // XPG + 1 < XPIECES:
                    load_x(g // XPG + 1)
                if g == 5:
                    sp.dma_start(w_in[:, :, :], wts).then_inc(w_loaded, 16)
            with sp.Fori(1, CHUNKS) as c:
                for g in range(GROUPS):
                    load_group(c, g)

        @block.gpsimd
        def _(pool):
            nc.gpsimd.memset(ln_eps[:, :], EPS).then_inc(ln_eps_ready, 1)
            pool.dma_start(bias_sb[:, :], bias).then_inc(small_loaded, 16)
            pool.dma_start(eps_sb[:, :], eps.to_broadcast([P, 2])).then_inc(small_loaded, 16)
            pool.dma_start(bm_sb[:, :], bm.to_broadcast([P, D])).then_inc(bm_loaded, 16)
            pool.wait_ge(bm_loaded, 16)
            pool.wait_ge(x_hi_ready, 2 * XPIECES)
            pool.wait_ge(x_lo_ready, 2 * XPIECES)
            for t in range(T):
                nc.gpsimd.tensor_tensor(x1_sb[:, t * D:(t + 1) * D], x1_sb[:, t * D:(t + 1) * D], bm_sb[:, :],
                                        ALU.add).then_inc(residual_ready, 1)
            with pool.Fori(0, CHUNKS) as m:
                pool.wait_ge(norm_ready, (m + 1) * TILES)
                pool.dma_start(out_chunks[:, bass.ds(m, 1), :], normed[:, :]).then_inc(stored, 16)
            pool.wait_ge(stored, 16 * CHUNKS)

        @block.tensor
        def _(pe):
            def accumulate(b, c, g):
                if b == 0:
                    pe.wait_ge(a_lo_ready, c * GROUPS + g + 1)
                if isinstance(c, int) and c == 0:
                    if g % XPG == 0:
                        pe.wait_ge(x_lo_ready, 2 * (g // XPG) + b + 1)
                elif g == 0:
                    pe.wait_ge(h_ready[b], (c - 1) * (LAYERS + 1) + 1)
                s = g % RING
                for u in range(GSLOTS):
                    t = g * GSLOTS + u
                    wh = x_hi[:, b, t * D:(t + 1) * D]
                    wl = x_lo[:, b, t * D:(t + 1) * D]
                    ah = a_hi[:, s, u * COLS:(u + 1) * COLS]
                    al = a_lo[:, s, u * COLS:(u + 1) * COLS]
                    nc.tensor.matmul(acc[b][:, :], wh, ah, start=(t == 0), stop=False)
                    nc.tensor.matmul(acc[b][:, :], wh, al, start=False, stop=False)
                    last = nc.tensor.matmul(acc[b][:, :], wl, ah, start=False, stop=(t == T - 1))
                return last

            def layer(b, m, l):
                pe.wait_ge(w_lo_ready, 1)
                pe.wait_ge(h_lo_ready[b], m * (LAYERS + 1) + l + 1)
                k = b * LAYERS + l
                nc.tensor.matmul(mlp[b][:, :], w_hi[:, k, :], h_hi[:, b, :], start=True, stop=False)
                nc.tensor.matmul(mlp[b][:, :], w_hi[:, k, :], h_lo[:, b, :], start=False, stop=False)
                nc.tensor.matmul(mlp[b][:, :], w_lo[:, k, :], h_hi[:, b, :], start=False,
                                 stop=True).then_inc(layer_done[b], 1)

            def merge(m):
                for b in range(2):
                    pe.wait_ge(h_lo_ready[b], (m + 1) * (LAYERS + 1))
                for j in range(TILES):
                    o = merged[:, j * D:(j + 1) * D]
                    for b in range(2):
                        k = 2 * LAYERS + b
                        hh = h_hi[:, b, j * P:(j + 1) * P]
                        hl = h_lo[:, b, j * P:(j + 1) * P]
                        nc.tensor.matmul(o, hh, w_hi[:, k, :], start=(b == 0), stop=False)
                        nc.tensor.matmul(o, hh, w_lo[:, k, :], start=False, stop=False)
                        last = nc.tensor.matmul(o, hl, w_hi[:, k, :], start=False, stop=(b == 1))
                last.then_inc(merge_done, 1)

            def mlp_step(m, s):
                if 3 <= s < 3 + 2 * LAYERS:
                    layer((s - 3) % 2, m, (s - 3) // 2)
                if s == 10:
                    merge(m)

            def chunk(c, m):
                for s in range(STEPS):
                    if s < GROUPS:
                        last = accumulate(0, c, s)
                        if s == GROUPS - 1:
                            last.then_inc(acc1_done, 1)
                    if s >= LAG:
                        accumulate(1, c, s - LAG).then_inc(group_used, 1)
                    if m is not None:
                        mlp_step(m, s)

            chunk(0, None)
            with pe.Fori(1, CHUNKS) as c:
                chunk(c, c - 1)
            for s in range(STEPS):
                mlp_step(CHUNKS - 1, s)

        @block.scalar
        def _(act):
            def x_high(j, b):
                if b == 0:
                    act.wait_ge(x_loaded[j % 2], 32 * (j // 2 + 1))
                src = x1_sb[:, j * XCOLS:(j + 1) * XCOLS] if b == 0 else x2_in[:, j % 2, :]
                nc.scalar.copy(x_hi[:, b, j * XCOLS:(j + 1) * XCOLS], src).then_inc(x_hi_ready, 1)

            def a_high(c, g):
                s = g % RING
                act.wait_ge(a_loaded[g % LOADS], c * (16 * GROUPS // LOADS) + 16 * (g // LOADS + 1))
                if not (isinstance(c, int) and c == 0 and g < RING):
                    act.wait_ge(group_used, c * GROUPS + (g - RING + 1))
                nc.scalar.copy(a_hi[:, s, :], a_in[:, g % LOADS, :]).then_inc(a_hi_ready, 1)

            def take_acc(b, m):
                if b == 0:
                    act.wait_ge(acc1_done, m + 1)
                else:
                    act.wait_ge(group_used, (m + 1) * GROUPS)
                nc.scalar.activation(h[:, b, :], acc[b][:, :], ACT.Copy,
                                     scale=gain[:, b:b + 1]).then_inc(h_ready[b], 1)

            def take_layer(b, m, l):
                act.wait_ge(layer_done[b], m * LAYERS + l + 1)
                k = b * LAYERS + l
                nc.scalar.activation(h[:, b, :], mlp[b][:, :], ACT.Relu,
                                     bias=bias_sb[:, k:k + 1]).then_inc(h_ready[b], 1)

            def deviation(m):
                act.wait_ge(var_ready, (m + 1) * TILES)
                nc.scalar.activation(std[:, :], mv[:, :, 1], ACT.Sqrt, bias=ln_eps[:, 0:1]).then_inc(std_ready, 1)

            def mlp_step(m, g):
                if g == 1:
                    take_acc(0, m)
                if g == 4:
                    take_acc(1, m)
                if 6 <= g < 6 + 2 * LAYERS:
                    take_layer((g - 6) % 2, m, (g - 6) // 2)
                if g == 14:
                    deviation(m)

            for g in range(GROUPS):
                if g % XPG == 0:
                    x_high(g // XPG, 0)
                a_high(0, g)
                if g % XPG == 0:
                    x_high(g // XPG, 1)
                if g == 8:
                    act.wait_ge(w_loaded, 16)
                    nc.scalar.copy(w_hi[:, :, :], w_in[:, :, :]).then_inc(w_hi_ready, 1)
            act.wait_ge(ln_eps_ready, 1)
            act.wait_ge(gain_ready, 1)
            with act.Fori(1, CHUNKS) as c:
                for g in range(GROUPS):
                    a_high(c, g)
                    mlp_step(c - 1, g)
            for g in range(GROUPS):
                mlp_step(CHUNKS - 1, g)

        @block.vector
        def _(dve):
            def x_low(j, b):
                dve.wait_ge(x_hi_ready, 2 * j + b + 1)
                cols = slice(j * XCOLS, (j + 1) * XCOLS)
                src = x1_sb[:, cols] if b == 0 else x2_in[:, j % 2, :]
                nc.vector.tensor_tensor(x_lo[:, b, cols], src, x_hi[:, b, cols].bitcast(F32),
                                        ALU.subtract).then_inc(x_lo_ready, 1)

            def a_low(c, g):
                s = g % RING
                dve.wait_ge(a_hi_ready, c * GROUPS + g + 1)
                nc.vector.tensor_tensor(a_lo[:, s, :], a_in[:, g % LOADS, :], a_hi[:, s, :].bitcast(F32),
                                        ALU.subtract).then_inc(a_lo_ready, 1)

            def split_h(b, m, n):
                count = m * (LAYERS + 1) + n + 1
                dve.wait_ge(h_ready[b], count)
                nc.vector.tensor_copy(h_hi[:, b, :], h[:, b, :]).then_inc(h_hi_ready[b], 1)
                dve.wait_ge(h_hi_ready[b], count)
                nc.vector.tensor_tensor(h_lo[:, b, :], h[:, b, :], h_hi[:, b, :].bitcast(F32),
                                        ALU.subtract).then_inc(h_lo_ready[b], 1)

            def statistics(m):
                dve.wait_ge(merge_done, m + 1)
                nc.vector.tensor_tensor(y[:, :], merged[:, :], x1_sb[:, bass.ds(m * COLS, COLS)],
                                        ALU.add).then_inc(y_ready, 1)
                dve.wait_ge(y_ready, m + 1)
                for j in range(TILES):
                    nc.vector.bn_stats(stats[:, j, :], y[:, j * D:(j + 1) * D]).then_inc(stats_ready, 1)
                dve.wait_ge(stats_ready, (m + 1) * TILES)

            def variances(m):
                for j in range(TILES):
                    nc.vector.bn_aggr(mv[:, j, :], stats[:, j, :]).then_inc(var_ready, 1)

            def normalise(m):
                dve.wait_ge(std_ready, m + 1)
                nc.vector.reciprocal(rstd[:, :], std[:, :]).then_inc(rstd_ready, 1)
                dve.wait_ge(rstd_ready, m + 1)
                dve.wait_ge(stored, m * 16)
                for j in range(TILES):
                    nc.vector.tensor_scalar(normed[:, j * D:(j + 1) * D], y[:, j * D:(j + 1) * D],
                                            mv[:, j, 0:1], rstd[:, j:j + 1], ALU.subtract,
                                            ALU.mult).then_inc(norm_ready, 1)

            def mlp_step(m, g):
                if g == 1:
                    split_h(0, m, 0)
                if g == 4:
                    split_h(1, m, 0)
                if 6 <= g < 6 + 2 * LAYERS:
                    split_h((g - 6) % 2, m, (g - 6) // 2 + 1)
                if g == 13:
                    statistics(m)
                if g == 14:
                    variances(m)
                if g == 15:
                    normalise(m)

            for g in range(GROUPS):
                if g % XPG == 0:
                    x_low(g // XPG, 0)
                a_low(0, g)
                if g % XPG == 0:
                    x_low(g // XPG, 1)
                if g == 6:
                    dve.wait_ge(small_loaded, 32)
                    nc.vector.tensor_scalar(gain[:, :], eps_sb[:, :], 1.0, 1.0, ALU.add,
                                            ALU.add).then_inc(gain_ready, 1)
                if g == 9:
                    dve.wait_ge(w_hi_ready, 1)
                    nc.vector.tensor_tensor(w_lo[:, :, :], w_in[:, :, :], w_hi[:, :, :].bitcast(F32),
                                            ALU.subtract).then_inc(w_lo_ready, 1)
            dve.wait_ge(residual_ready, T)
            with dve.Fori(1, CHUNKS) as c:
                for g in range(GROUPS):
                    a_low(c, g)
                    mlp_step(c - 1, g)
            for g in range(GROUPS):
                mlp_step(CHUNKS - 1, g)


def kernel(x, adj, L0_gnn_x2, L0_gnn_eps1, L0_gnn_eps2, L0_gnn_W1, L0_gnn_b1, L0_gnn_W2, L0_gnn_b2,
           L0_gnn_Wm, L0_gnn_bm):
    import numpy as np
    import concourse.bacc as bacc
    from concourse.bass_utils import run_bass_kernel_spmd

    f = np.ascontiguousarray
    a = np.asarray(adj).reshape(P, CHUNKS, TILES, P, GROUPS, GSLOTS)
    a = f(a.transpose(1, 4, 3, 5, 2, 0)).reshape(CHUNKS, GROUPS, P, GCOLS)
    w1, w2, wm = np.asarray(L0_gnn_W1), np.asarray(L0_gnn_W2), np.asarray(L0_gnn_Wm)
    w = f(np.concatenate([w1, w2, wm.reshape(D, 2, D).transpose(1, 0, 2)]).transpose(2, 0, 1))
    b = f(np.concatenate([np.asarray(L0_gnn_b1), np.asarray(L0_gnn_b2)]).T)
    e = np.concatenate([np.asarray(L0_gnn_eps1), np.asarray(L0_gnn_eps2)]).reshape(1, 2)
    arrays = {"x1": f(x), "x2": f(L0_gnn_x2), "adj_t": a, "wts": w, "bias": b, "eps": f(e),
              "bm": f(L0_gnn_bm).reshape(1, D)}

    nc = bacc.Bacc("TRN2", target_bir_lowering=False, num_devices=1)
    ins = [nc.dram_tensor(k, v.shape, mybir.dt.from_np(v.dtype), kind="ExternalInput").ap()
           for k, v in arrays.items()]
    out = nc.dram_tensor("out", (N, D), F32, kind="ExternalOutput").ap()
    build(nc, *ins, out)
    r = run_bass_kernel_spmd(nc, [arrays], core_ids=[0])
    return r.results[0]["out"]
```

```python
from contextlib import ExitStack

import concourse.bass as bass
from concourse import mybir

ALU = mybir.AluOpType
ACT = mybir.ActivationFunctionType
F32 = mybir.dt.float32
F32R = mybir.dt.float32r

P = 128
N = 4096
D = 128
LAYERS = 3
T = N // P
COLS = 512
HALF = COLS // 2
CHUNKS = N // COLS
LAST = CHUNKS - 1
TILES = COLS // P
GSLOTS = 2
GROUPS = T // GSLOTS
GCOLS = GSLOTS * COLS
RING = 8
LOADS = 4
XSLOTS = 4
XPIECES = T // XSLOTS
XCOLS = XSLOTS * D
XPG = XSLOTS // GSLOTS
EPS = 1e-5
NW = 2 * LAYERS + 2
STAGES = LAYERS + 1
LAGS = [3] * GROUPS
FIRST_LAGS = [0] * 8 + [1, 1, 2, 2] + [3] * 4
LAST_LAGS = [3] * 12 + [4, 5, 6, 6]
EARLY = (4, 2, 0)
WARM = 8
TAIL = ([(0, 0, None), (0, 1, None), (0, 2, None), (1, 0, 0), (1, 0, 1), (0, 3, None)]
        + [(1, n, half) for n in range(1, STAGES) for half in range(2)])


def columns(half):
    return slice(0, COLS) if half is None else slice(half * HALF, (half + 1) * HALF)


def tiles_of(half):
    cols = columns(half)
    return slice(cols.start // P, cols.stop // P)


def count(m, per_chunk, n, half):
    return m * per_chunk + (n + 1 if half is None else 2 * n + half + 1)


def build(nc, x1, x2, adj, wts, bias, eps, bm, out):
    with ExitStack() as ctx:
        def sb(name, shape, dt=F32):
            return ctx.enter_context(nc.sbuf_tensor(name, shape, dt))

        def pb(name):
            return ctx.enter_context(nc.psum_tensor(name, [P, COLS], F32))

        def sem(name):
            return ctx.enter_context(nc.semaphore(name))

        x1_sb = sb("x1_sb", [P, T * D])
        x2_in = sb("x2_in", [P, 2, XCOLS])
        x_hi = sb("x_hi", [P, 2, T * D], F32R)
        x_lo = sb("x_lo", [P, 2, T * D], F32R)
        a_in = sb("a_in", [P, LOADS, GCOLS])
        a_hi = sb("a_hi", [P, RING, GCOLS], F32R)
        a_lo = sb("a_lo", [P, RING, GCOLS], F32R)
        w_in = sb("w_in", [P, NW, D])
        w_hi = sb("w_hi", [P, NW, D], F32R)
        w_lo = sb("w_lo", [P, NW, D], F32R)
        bias_sb = sb("bias_sb", [P, 2 * LAYERS])
        eps_sb = sb("eps_sb", [P, 2])
        gain = sb("gain", [P, 2])
        bm_sb = sb("bm_sb", [P, 1])
        ident = sb("ident", [P, P])
        ln_eps = sb("ln_eps", [P, 1])
        zeros = sb("zeros", [P, COLS], F32R)
        h = sb("h", [P, 2, COLS])
        h_hi = sb("h_hi", [P, 2, COLS], F32R)
        h_lo = sb("h_lo", [P, 2, COLS], F32R)
        merged_sb = sb("merged_sb", [P, COLS])
        y = sb("y", [P, COLS])
        stats = sb("stats", [P, TILES, 6])
        mv = sb("mv", [P, TILES, 2])
        std = sb("std", [P, TILES])
        rstd = sb("rstd", [P, TILES])
        normed = sb("normed", [P, COLS])

        acc = [pb(f"acc{b}") for b in range(2)]
        mlp = [pb(f"mlp{b}") for b in range(2)]
        merged = pb("merged")
        turned = pb("turned")
        spare = pb("spare")
        mlp2_half = [mlp[1], spare]
        merged_half = [merged, mlp[0]]
        turned_half = [turned, acc[0]]

        a_loaded = [sem(f"a_loaded{s}") for s in range(LOADS)]
        first_loaded = sem("first_loaded")
        x_loaded = [[sem(f"x{b + 1}_loaded{s}") for s in range(2)] for b in range(2)]
        w_loaded = sem("w_loaded")
        small_loaded = sem("small_loaded")
        first_hi_ready = sem("first_hi_ready")
        first_lo_ready = sem("first_lo_ready")
        a_hi_ready = sem("a_hi_ready")
        a_lo_ready = sem("a_lo_ready")
        x_hi_ready = sem("x_hi_ready")
        x_lo_ready = sem("x_lo_ready")
        w_hi_ready = sem("w_hi_ready")
        w_lo_ready = sem("w_lo_ready")
        zeros_ready = sem("zeros_ready")
        gain_ready = sem("gain_ready")
        ln_eps_ready = sem("ln_eps_ready")
        ident_zero = sem("ident_zero")
        ident_ready = sem("ident_ready")
        acc1_done = sem("acc1_done")
        group_used = sem("group_used")
        layer_done = [sem(f"layer_done{b}") for b in range(2)]
        h_ready = [sem(f"h_ready{b}") for b in range(2)]
        h_hi_ready = [sem(f"h_hi_ready{b}") for b in range(2)]
        h_lo_ready = [sem(f"h_lo_ready{b}") for b in range(2)]
        merge_done = sem("merge_done")
        merged_ready = sem("merged_ready")
        turn_done = sem("turn_done")
        y_ready = sem("y_ready")
        stats_ready = sem("stats_ready")
        var_ready = sem("var_ready")
        std_ready = sem("std_ready")
        rstd_ready = sem("rstd_ready")
        norm_ready = sem("norm_ready")
        stored = sem("stored")
        normed_free = sem("normed_free")
        last_stored = sem("last_stored")

        adj_rows = adj.rearrange("c g p n -> (c g p) n")
        x_pieces = [x.rearrange("(p j t) d -> j p (t d)", p=P, j=XPIECES) for x in (x1, x2)]
        out_chunks = out.rearrange("(p c t) d -> p c (t d)", p=P, c=CHUNKS)

        block = ctx.enter_context(nc.Block())

        @block.sync
        def _(sp):
            def load_group(c, g):
                if isinstance(c, int):
                    if g >= LOADS:
                        sp.wait_ge(a_lo_ready, g - LOADS + 1)
                else:
                    sp.wait_ge(a_lo_ready, c * GROUPS + (g - LOADS + 1))
                sp.dma_start(a_in[:, g % LOADS, :],
                             adj_rows[bass.ds((c * GROUPS + g) * P, P), :]).then_inc(a_loaded[g % LOADS], 16)

            def load_x(j, b):
                if j >= 2:
                    sp.wait_ge(x_lo_ready, 2 * (j - 2) + b + 1)
                dst = x1_sb[:, j * XCOLS:(j + 1) * XCOLS] if b == 0 else x2_in[:, j % 2, :]
                sp.dma_start(dst, x_pieces[b][j]).then_inc(x_loaded[b][j % 2], 16)

            load_x(0, 0)
            sp.dma_start(a_in[:, 0, 0:COLS], adj_rows[0:P, 0:COLS]).then_inc(first_loaded, 16)
            sp.dma_start(a_in[:, 0, COLS:GCOLS], adj_rows[0:P, COLS:GCOLS]).then_inc(a_loaded[0], 16)
            load_x(0, 1)
            for g in range(1, GROUPS):
                load_group(0, g)
                if g % XPG == 1 and g // XPG + 1 < XPIECES:
                    load_x(g // XPG + 1, 0)
                    load_x(g // XPG + 1, 1)
                if g == 5:
                    sp.dma_start(w_in[:, :, :], wts).then_inc(w_loaded, 16)
            with sp.Fori(1, CHUNKS) as c:
                for g in range(GROUPS):
                    load_group(c, g)
            for half in range(2):
                sp.wait_ge(norm_ready, LAST * TILES + tiles_of(half).stop)
                sp.dma_start(out_chunks[:, LAST, columns(half)], normed[:, columns(half)]).then_inc(last_stored, 16)
            sp.wait_ge(last_stored, 32)

        @block.gpsimd
        def _(pool):
            pool.dma_start(bias_sb[:, :], bias).then_inc(small_loaded, 16)
            pool.dma_start(eps_sb[:, :], eps.to_broadcast([P, 2])).then_inc(small_loaded, 16)
            pool.dma_start(bm_sb[:, :], bm).then_inc(small_loaded, 16)
            nc.gpsimd.memset(ln_eps[:, :], EPS).then_inc(ln_eps_ready, 1)
            nc.gpsimd.memset(ident[:, :], 0.0).then_inc(ident_zero, 1)
            pool.wait_ge(ident_zero, 1)
            nc.gpsimd.affine_select(out=ident[:, :], in_=ident[:, :], compare_op=ALU.not_equal, fill=1.0,
                                    base=0, pattern=[[-1, P]], channel_multiplier=1).then_inc(ident_ready, 1)
            pool.sem_inc(normed_free, 1)
            with pool.Fori(0, LAST) as m:
                pool.wait_ge(norm_ready, (m + 1) * TILES)
                pool.dma_start(out_chunks[:, bass.ds(m, 1), :], normed[:, :]).then_inc(stored, 16)
                pool.wait_ge(stored, (m + 1) * 16)
                pool.sem_inc(normed_free, 1)

        @block.tensor
        def _(pe):
            def accumulate(b, c, g):
                first = isinstance(c, int) and c == 0
                if first:
                    if b == 0 and g > 0:
                        pe.wait_ge(a_lo_ready, g + 1)
                    if g % XPG == 0:
                        pe.wait_ge(x_lo_ready, 2 * (g // XPG) + b + 1)
                else:
                    if b == 0 and g % 2 == 0:
                        pe.wait_ge(a_lo_ready, c * GROUPS + g + 2)
                    if g == 0:
                        pe.wait_ge(h_ready[b], (c - 1) * STAGES + 1)
                s = g % RING
                for u in range(GSLOTS):
                    t = g * GSLOTS + u
                    if first and b == 0 and g == 0:
                        pe.wait_ge(a_lo_ready if u else first_lo_ready, 1)
                    xh = x_hi[:, b, t * D:(t + 1) * D]
                    xl = x_lo[:, b, t * D:(t + 1) * D]
                    ah = a_hi[:, s, u * COLS:(u + 1) * COLS]
                    al = a_lo[:, s, u * COLS:(u + 1) * COLS]
                    nc.tensor.matmul(acc[b][:, :], xh, ah, start=(t == 0), stop=False)
                    nc.tensor.matmul(acc[b][:, :], xh, al, start=False, stop=False)
                    last = nc.tensor.matmul(acc[b][:, :], xl, ah, start=False, stop=(t == T - 1))
                return last

            def weigh(bank, k, b, start, stop, half=None):
                cols = columns(half)
                hh, hl, o = h_hi[:, b, cols], h_lo[:, b, cols], bank[:, cols]
                nc.tensor.matmul(o, w_hi[:, k, :], hh, start=start, stop=False)
                nc.tensor.matmul(o, w_hi[:, k, :], hl, start=False, stop=False)
                return nc.tensor.matmul(o, w_lo[:, k, :], hh, start=False, stop=stop)

            def layer(b, m, l, half=None):
                pe.wait_ge(h_lo_ready[b], count(m, STAGES, l, half))
                bank = mlp[b] if half is None else mlp2_half[half]
                weigh(bank, b * LAYERS + l, b, True, True, half).then_inc(layer_done[b], 1)

            def merge(b, m, half=None):
                pe.wait_ge(h_lo_ready[b], count(m, STAGES, LAYERS, half if b else None))
                bank = merged if half is None else merged_half[half]
                last = weigh(bank, 2 * LAYERS + b, b, b == 0, b == 1, half)
                if b == 1:
                    last.then_inc(merge_done, 1)

            def turn(m, half=None):
                pe.wait_ge(merged_ready, count(m, 1, 0, half))
                bank = turned if half is None else turned_half[half]
                cols = columns(half)
                for j in range(cols.start, cols.stop, P):
                    last = nc.tensor.transpose(bank[:, j:j + P], merged_sb[:, j:j + P], ident[:, :])
                last.then_inc(turn_done, 1)

            def mlp_step(m, s):
                if 2 <= s < 2 + 2 * LAYERS:
                    layer((s - 2) % 2, m, (s - 2) // 2)
                if s == 9:
                    merge(0, m)
                    merge(1, m)
                if s == 11:
                    turn(m)

            def chunk(c, m, lags, after=lambda left: None):
                behind = 0
                for s in range(GROUPS):
                    last = accumulate(0, c, s)
                    if s == GROUPS - 1:
                        last.then_inc(acc1_done, 1)
                    while behind <= s - lags[s]:
                        accumulate(1, c, behind).then_inc(group_used, 1)
                        behind += 1
                    if m is not None:
                        mlp_step(m, s)
                for g in range(behind, GROUPS):
                    accumulate(1, c, g).then_inc(group_used, 1)
                    after(GROUPS - 1 - g)

            def early_layers(left):
                if left in EARLY:
                    layer(0, LAST, EARLY.index(left))

            pe.wait_ge(zeros_ready, 1)
            for _ in range(WARM):
                nc.tensor.matmul(spare[:, :], zeros[:, 0:P], zeros[:, :], start=True, stop=True)
            chunk(0, None, FIRST_LAGS)
            pe.wait_ge(w_lo_ready, 1)
            pe.wait_ge(ident_ready, 1)
            with pe.Fori(1, LAST) as c:
                chunk(c, c - 1, LAGS)
            chunk(LAST, LAST - 1, LAST_LAGS, early_layers)
            for l in range(LAYERS):
                if l == LAYERS - 1:
                    merge(0, LAST, 0)
                    merge(0, LAST, 1)
                for half in range(2):
                    layer(1, LAST, l, half)
            for half in range(2):
                merge(1, LAST, half)
            for half in range(2):
                turn(LAST, half)

        @block.scalar
        def _(act):
            def x_high(j, b):
                act.wait_ge(x_loaded[b][j % 2], 16 * (j // 2 + 1))
                src = x1_sb[:, j * XCOLS:(j + 1) * XCOLS] if b == 0 else x2_in[:, j % 2, :]
                nc.scalar.copy(x_hi[:, b, j * XCOLS:(j + 1) * XCOLS], src).then_inc(x_hi_ready, 1)

            def a_high(c, g):
                s = g % RING
                act.wait_ge(a_loaded[g % LOADS], c * (16 * GROUPS // LOADS) + 16 * (g // LOADS + 1))
                if not isinstance(c, int) or g >= RING:
                    act.wait_ge(group_used, c * GROUPS + (g - RING + 1))
                nc.scalar.copy(a_hi[:, s, :], a_in[:, g % LOADS, :]).then_inc(a_hi_ready, 1)

            def take_acc(b, m, half=None):
                if b == 0:
                    act.wait_ge(acc1_done, m + 1)
                else:
                    act.wait_ge(group_used, (m + 1) * GROUPS)
                cols = columns(half)
                nc.scalar.activation(h[:, b, cols], acc[b][:, cols], ACT.Copy,
                                     scale=gain[:, b:b + 1]).then_inc(h_ready[b], 1)

            def take_layer(b, m, l, half=None):
                act.wait_ge(layer_done[b], count(m, LAYERS, l, half))
                k = b * LAYERS + l
                cols = columns(half)
                bank = mlp[b] if half is None else mlp2_half[half]
                nc.scalar.activation(h[:, b, cols], bank[:, cols], ACT.Relu,
                                     bias=bias_sb[:, k:k + 1]).then_inc(h_ready[b], 1)

            def take_merged(m, half=None):
                act.wait_ge(merge_done, count(m, 1, 0, half))
                cols = columns(half)
                bank = merged if half is None else merged_half[half]
                nc.scalar.activation(merged_sb[:, cols], bank[:, cols], ACT.Identity,
                                     bias=bm_sb[:, 0:1]).then_inc(merged_ready, 1)

            def deviation(m, half=None):
                tiles = tiles_of(half)
                act.wait_ge(var_ready, m * TILES + tiles.stop)
                nc.scalar.activation(std[:, tiles], mv[:, tiles, 1], ACT.Sqrt,
                                     bias=ln_eps[:, 0:1]).then_inc(std_ready, 1)

            def mlp_step(m, g):
                if g == 1:
                    take_acc(0, m)
                if g == 3:
                    take_acc(1, m)
                if 4 <= g < 4 + 2 * LAYERS:
                    take_layer((g - 4) % 2, m, (g - 4) // 2)
                if g == 11:
                    take_merged(m)
                if g == 15:
                    deviation(m)

            x_high(0, 0)
            act.wait_ge(first_loaded, 16)
            nc.scalar.copy(a_hi[:, 0, 0:COLS], a_in[:, 0, 0:COLS]).then_inc(first_hi_ready, 1)
            act.wait_ge(a_loaded[0], 16)
            nc.scalar.copy(a_hi[:, 0, COLS:GCOLS], a_in[:, 0, COLS:GCOLS]).then_inc(a_hi_ready, 1)
            x_high(0, 1)
            for g in range(1, GROUPS):
                if g % XPG == 0:
                    x_high(g // XPG, 0)
                a_high(0, g)
                if g % XPG == 0:
                    x_high(g // XPG, 1)
                if g == 8:
                    act.wait_ge(w_loaded, 16)
                    nc.scalar.copy(w_hi[:, :, :], w_in[:, :, :]).then_inc(w_hi_ready, 1)
            act.wait_ge(ln_eps_ready, 1)
            act.wait_ge(gain_ready, 1)
            with act.Fori(1, CHUNKS) as c:
                for g in range(GROUPS):
                    a_high(c, g)
                    mlp_step(c - 1, g)
            for b, n, half in TAIL:
                if n == 0:
                    take_acc(b, LAST, half)
                else:
                    take_layer(b, LAST, n - 1, half)
            for half in range(2):
                take_merged(LAST, half)
            for half in range(2):
                deviation(LAST, half)

        @block.vector
        def _(dve):
            def x_low(j, b):
                dve.wait_ge(x_hi_ready, 2 * j + b + 1)
                cols = slice(j * XCOLS, (j + 1) * XCOLS)
                src = x1_sb[:, cols] if b == 0 else x2_in[:, j % 2, :]
                nc.vector.tensor_tensor(x_lo[:, b, cols], src, x_hi[:, b, cols].bitcast(F32),
                                        ALU.subtract).then_inc(x_lo_ready, 1)

            def a_low(c, g):
                s = g % RING
                dve.wait_ge(a_hi_ready, c * GROUPS + g + 1)
                nc.vector.tensor_tensor(a_lo[:, s, :], a_in[:, g % LOADS, :], a_hi[:, s, :].bitcast(F32),
                                        ALU.subtract).then_inc(a_lo_ready, 1)

            def split_h(b, m, n, half=None):
                cols = columns(half)
                done = count(m, STAGES, n, half)
                dve.wait_ge(h_ready[b], done)
                nc.vector.tensor_copy(h_hi[:, b, cols], h[:, b, cols]).then_inc(h_hi_ready[b], 1)
                dve.wait_ge(h_hi_ready[b], done)
                nc.vector.tensor_tensor(h_lo[:, b, cols], h[:, b, cols], h_hi[:, b, cols].bitcast(F32),
                                        ALU.subtract).then_inc(h_lo_ready[b], 1)

            def statistics(m, half=None):
                cols, tiles = columns(half), tiles_of(half)
                dve.wait_ge(turn_done, count(m, 1, 0, half))
                bank = turned if half is None else turned_half[half]
                x = x1_sb[:, bass.ds(m * COLS + cols.start, cols.stop - cols.start)]
                nc.vector.tensor_tensor(y[:, cols], bank[:, cols], x, ALU.add).then_inc(y_ready, 1)
                dve.wait_ge(y_ready, count(m, 1, 0, half))
                for j in range(tiles.start, tiles.stop):
                    nc.vector.bn_stats(stats[:, j, :], y[:, j * D:(j + 1) * D]).then_inc(stats_ready, 1)
                dve.wait_ge(stats_ready, m * TILES + tiles.stop)

            def variances(m, half=None):
                tiles = tiles_of(half)
                for j in range(tiles.start, tiles.stop):
                    nc.vector.bn_aggr(mv[:, j, :], stats[:, j, :]).then_inc(var_ready, 1)

            def normalise(m, half=None):
                tiles = tiles_of(half)
                dve.wait_ge(std_ready, count(m, 1, 0, half))
                nc.vector.reciprocal(rstd[:, tiles], std[:, tiles]).then_inc(rstd_ready, 1)
                dve.wait_ge(rstd_ready, count(m, 1, 0, half))
                if half != 1:
                    dve.wait_ge(normed_free, m + 1)
                for j in range(tiles.start, tiles.stop):
                    nc.vector.tensor_scalar(normed[:, j * D:(j + 1) * D], y[:, j * D:(j + 1) * D],
                                            mv[:, j, 0:1], rstd[:, j:j + 1], ALU.subtract,
                                            ALU.mult).then_inc(norm_ready, 1)

            def mlp_step(m, g):
                if g == 1:
                    split_h(0, m, 0)
                if g == 3:
                    split_h(1, m, 0)
                if 4 <= g < 4 + 2 * LAYERS:
                    split_h((g - 4) % 2, m, (g - 4) // 2 + 1)
                if g == 13:
                    statistics(m)
                if g == 14:
                    variances(m)
                if g == 15:
                    normalise(m)

            nc.vector.memset(zeros[:, :].bitcast(F32), 0.0).then_inc(zeros_ready, 1)
            x_low(0, 0)
            dve.wait_ge(first_hi_ready, 1)
            nc.vector.tensor_tensor(a_lo[:, 0, 0:COLS], a_in[:, 0, 0:COLS], a_hi[:, 0, 0:COLS].bitcast(F32),
                                    ALU.subtract).then_inc(first_lo_ready, 1)
            dve.wait_ge(a_hi_ready, 1)
            nc.vector.tensor_tensor(a_lo[:, 0, COLS:GCOLS], a_in[:, 0, COLS:GCOLS],
                                    a_hi[:, 0, COLS:GCOLS].bitcast(F32), ALU.subtract).then_inc(a_lo_ready, 1)
            x_low(0, 1)
            for g in range(1, GROUPS):
                if g % XPG == 0:
                    x_low(g // XPG, 0)
                a_low(0, g)
                if g % XPG == 0:
                    x_low(g // XPG, 1)
                if g == 6:
                    dve.wait_ge(small_loaded, 48)
                    nc.vector.tensor_scalar(gain[:, :], eps_sb[:, :], 1.0, 1.0, ALU.add,
                                            ALU.add).then_inc(gain_ready, 1)
                if g == 9:
                    dve.wait_ge(w_hi_ready, 1)
                    nc.vector.tensor_tensor(w_lo[:, :, :], w_in[:, :, :], w_hi[:, :, :].bitcast(F32),
                                            ALU.subtract).then_inc(w_lo_ready, 1)
            with dve.Fori(1, CHUNKS) as c:
                for g in range(GROUPS):
                    a_low(c, g)
                    mlp_step(c - 1, g)
            for b, n, half in TAIL:
                split_h(b, LAST, n, half)
            for half in range(2):
                statistics(LAST, half)
                variances(LAST, half)
            for half in range(2):
                normalise(LAST, half)


def kernel(x, adj, L0_gnn_x2, L0_gnn_eps1, L0_gnn_eps2, L0_gnn_W1, L0_gnn_b1, L0_gnn_W2, L0_gnn_b2,
           L0_gnn_Wm, L0_gnn_bm):
    import numpy as np
    import concourse.bacc as bacc
    from concourse.bass_utils import run_bass_kernel_spmd

    f = np.ascontiguousarray
    a = np.asarray(adj).reshape(P, CHUNKS, TILES, P, GROUPS, GSLOTS)
    a = f(a.transpose(1, 4, 3, 5, 2, 0)).reshape(CHUNKS, GROUPS, P, GCOLS)
    w1, w2, wm = np.asarray(L0_gnn_W1), np.asarray(L0_gnn_W2), np.asarray(L0_gnn_Wm)
    w = f(np.concatenate([w1, w2, wm.reshape(D, 2, D).transpose(1, 0, 2)]).transpose(2, 0, 1))
    b = f(np.concatenate([np.asarray(L0_gnn_b1), np.asarray(L0_gnn_b2)]).T)
    e = np.concatenate([np.asarray(L0_gnn_eps1), np.asarray(L0_gnn_eps2)]).reshape(1, 2)
    arrays = {"x1": f(x), "x2": f(L0_gnn_x2), "adj_t": a, "wts": w, "bias": b, "eps": f(e),
              "bm": f(L0_gnn_bm).reshape(D, 1)}

    nc = bacc.Bacc("TRN2", target_bir_lowering=False, num_devices=1)
    ins = [nc.dram_tensor(k, v.shape, mybir.dt.from_np(v.dtype), kind="ExternalInput").ap()
           for k, v in arrays.items()]
    out = nc.dram_tensor("out", (N, D), F32, kind="ExternalOutput").ap()
    build(nc, *ins, out)
    r = run_bass_kernel_spmd(nc, [arrays], core_ids=[0])
    return r.results[0]["out"]
```

```python
from contextlib import ExitStack

import concourse.bass as bass
from concourse import mybir

ALU = mybir.AluOpType
ACT = mybir.ActivationFunctionType
F32 = mybir.dt.float32
F32R = mybir.dt.float32r

P = 128
N = 4096
D = 128
LAYERS = 3
T = N // P
COLS = 512
HALF = COLS // 2
CHUNKS = N // COLS
LAST = CHUNKS - 1
TILES = COLS // P
GSLOTS = 2
GROUPS = T // GSLOTS
GCOLS = GSLOTS * COLS
RING = 8
LOADS = 4
XSLOTS = 4
XPIECES = T // XSLOTS
XCOLS = XSLOTS * D
XPG = XSLOTS // GSLOTS
EPS = 1e-5
NW = 2 * LAYERS + 2
ROW = LAYERS * D + HALF
STAGES = LAYERS + 1
LAGS = [3] * GROUPS
FIRST_LAGS = [0] * 13 + [1, 2, 3]
LAST_LAGS = [3] * 12 + [4, 5, 6, 6]
BY_SLOT = 4
NORM_STEP = 13
EARLY = (4, 2, 0)
WARM = 8
TAIL = ([(0, 0, None), (0, 1, None), (0, 2, None), (1, 0, None), (0, 3, None)]
        + [(1, n, half) for n in range(1, STAGES) for half in range(2)])


def columns(half):
    return slice(0, COLS) if half is None else slice(half * HALF, (half + 1) * HALF)


def tiles_of(half):
    cols = columns(half)
    return slice(cols.start // P, cols.stop // P)


def count(m, per_chunk, n, half):
    return m * per_chunk + (n + 1 if half is None else 2 * n + half + 1)


def half_hi_count(n, half):
    return 1 if n == 0 else 2 * n + half


def build(nc, x1, x2, adj, wts, bias, eps, bias_row, bm, out):
    with ExitStack() as ctx:
        def sb(name, shape, dt=F32):
            return ctx.enter_context(nc.sbuf_tensor(name, shape, dt))

        def pb(name):
            return ctx.enter_context(nc.psum_tensor(name, [P, COLS], F32))

        def sem(name):
            return ctx.enter_context(nc.semaphore(name))

        x1_sb = sb("x1_sb", [P, T * D])
        x2_in = sb("x2_in", [P, 2, XCOLS])
        x_hi = sb("x_hi", [P, 2, T * D], F32R)
        x_lo = sb("x_lo", [P, 2, T * D], F32R)
        a_in = sb("a_in", [P, LOADS, GCOLS])
        a_hi = sb("a_hi", [P, RING, GCOLS], F32R)
        a_lo = sb("a_lo", [P, RING, GCOLS], F32R)
        w_in = sb("w_in", [P, NW, D])
        w_hi = sb("w_hi", [P, NW, D], F32R)
        w_lo = sb("w_lo", [P, NW, D], F32R)
        bias_sb = sb("bias_sb", [P, 2 * LAYERS])
        row_in = sb("row_in", [1, ROW])
        row_hi = sb("row_hi", [1, ROW], F32R)
        row_lo = sb("row_lo", [1, ROW], F32R)
        ones = sb("ones", [1, HALF], F32R)
        eps_sb = sb("eps_sb", [P, 2])
        gain = sb("gain", [P, 2])
        bm_sb = sb("bm_sb", [P, 1])
        ident = sb("ident", [P, P])
        ln_eps = sb("ln_eps", [P, 1])
        zeros = sb("zeros", [P, COLS], F32R)
        h = sb("h", [P, 2, COLS])
        h_hi = sb("h_hi", [P, 2, COLS], F32R)
        h_lo = sb("h_lo", [P, 2, COLS], F32R)
        merged_sb = sb("merged_sb", [P, COLS])
        y = sb("y", [P, COLS])
        stats = sb("stats", [P, TILES, 6])
        mv = sb("mv", [P, TILES, 2])
        std = sb("std", [P, TILES])
        rstd = sb("rstd", [P, TILES])
        var_rstd = sb("var_rstd", [P, TILES])
        half_square = sb("half_square", [P, TILES])
        scale = sb("scale", [P, TILES])
        normed = sb("normed", [P, COLS])

        acc = [pb(f"acc{b}") for b in range(2)]
        mlp = [pb(f"mlp{b}") for b in range(2)]
        merged = pb("merged")
        turned = pb("turned")
        spare = pb("spare")
        spare2 = pb("spare2")
        mlp2_half = [[mlp[1], spare], [turned, acc[0]], [acc[1], spare2]]
        rows_half = [merged, mlp[0]]

        a_loaded = [sem(f"a_loaded{s}") for s in range(LOADS)]
        first_loaded = [sem(f"first_loaded{g}") for g in range(BY_SLOT)]
        x_loaded = [[sem(f"x{b + 1}_loaded{s}") for s in range(2)] for b in range(2)]
        w_loaded = sem("w_loaded")
        small_loaded = sem("small_loaded")
        first_hi_ready = sem("first_hi_ready")
        first_lo_ready = sem("first_lo_ready")
        a_hi_ready = sem("a_hi_ready")
        a_lo_ready = sem("a_lo_ready")
        x_hi_ready = sem("x_hi_ready")
        x_lo_ready = sem("x_lo_ready")
        w_hi_ready = sem("w_hi_ready")
        w_lo_ready = sem("w_lo_ready")
        row_hi_ready = sem("row_hi_ready")
        row_lo_ready = sem("row_lo_ready")
        zeros_ready = sem("zeros_ready")
        ones_ready = sem("ones_ready")
        gain_ready = sem("gain_ready")
        ln_eps_ready = sem("ln_eps_ready")
        ident_zero = sem("ident_zero")
        ident_ready = sem("ident_ready")
        acc1_done = sem("acc1_done")
        group_used = sem("group_used")
        layer_done = [sem(f"layer_done{b}") for b in range(2)]
        h_ready = [sem(f"h_ready{b}") for b in range(2)]
        h_hi_ready = [sem(f"h_hi_ready{b}") for b in range(2)]
        h_lo_ready = [sem(f"h_lo_ready{b}") for b in range(2)]
        half_hi_ready = sem("half_hi_ready")
        merge_done = sem("merge_done")
        merged_ready = sem("merged_ready")
        rows_done = sem("rows_done")
        y_ready = sem("y_ready")
        stats_ready = sem("stats_ready")
        var_ready = sem("var_ready")
        std_ready = sem("std_ready")
        rstd_ready = sem("rstd_ready")
        refined = [sem(f"refined{k}") for k in range(3)]
        norm_ready = sem("norm_ready")
        stored = sem("stored")
        normed_free = sem("normed_free")
        last_stored = sem("last_stored")

        adj_rows = adj.rearrange("c g p n -> (c g p) n")
        x_pieces = [x.rearrange("(p j t) d -> j p (t d)", p=P, j=XPIECES) for x in (x1, x2)]
        out_chunks = out.rearrange("(p c t) d -> p c (t d)", p=P, c=CHUNKS)

        block = ctx.enter_context(nc.Block())

        @block.sync
        def _(sp):
            def load_group(c, g):
                if isinstance(c, int) and c == 0:
                    if g >= LOADS:
                        sp.wait_ge(a_lo_ready, g - LOADS + 1)
                else:
                    sp.wait_ge(a_lo_ready, c * GROUPS + (g - LOADS + 1))
                sp.dma_start(a_in[:, g % LOADS, :],
                             adj_rows[bass.ds((c * GROUPS + g) * P, P), :]).then_inc(a_loaded[g % LOADS], 16)

            def load_x(j, b):
                if j >= 2:
                    sp.wait_ge(x_lo_ready, 2 * (j - 2) + b + 1)
                dst = x1_sb[:, j * XCOLS:(j + 1) * XCOLS] if b == 0 else x2_in[:, j % 2, :]
                sp.dma_start(dst, x_pieces[b][j]).then_inc(x_loaded[b][j % 2], 16)

            load_x(0, 0)
            for g in range(GROUPS):
                if g < BY_SLOT:
                    for u, loaded in ((0, first_loaded[g]), (1, a_loaded[g])):
                        cols = slice(u * COLS, (u + 1) * COLS)
                        sp.dma_start(a_in[:, g, cols], adj_rows[g * P:(g + 1) * P, cols]).then_inc(loaded, 16)
                else:
                    load_group(0, g)
                if g == 0:
                    load_x(0, 1)
                elif g % XPG == 0:
                    load_x(g // XPG, 0)
                    load_x(g // XPG, 1)
                if g == 12:
                    sp.dma_start(w_in[:, :, :], wts).then_inc(w_loaded, 16)
            with sp.Fori(1, CHUNKS) as c:
                for g in range(GROUPS):
                    load_group(c, g)
            for half in range(2):
                sp.wait_ge(norm_ready, LAST * TILES + tiles_of(half).stop)
                sp.dma_start(out_chunks[:, LAST, columns(half)], normed[:, columns(half)]).then_inc(last_stored, 16)
            sp.wait_ge(last_stored, 32)

        @block.gpsimd
        def _(pool):
            pool.dma_start(bias_sb[:, :], bias).then_inc(small_loaded, 16)
            pool.dma_start(eps_sb[:, :], eps.to_broadcast([P, 2])).then_inc(small_loaded, 16)
            pool.dma_start(bm_sb[:, :], bm).then_inc(small_loaded, 16)
            pool.dma_start(row_in[:, :], bias_row).then_inc(small_loaded, 16)
            nc.gpsimd.memset(ln_eps[:, :], EPS).then_inc(ln_eps_ready, 1)
            nc.gpsimd.memset(ident[:, :], 0.0).then_inc(ident_zero, 1)
            pool.wait_ge(ident_zero, 1)
            nc.gpsimd.affine_select(out=ident[:, :], in_=ident[:, :], compare_op=ALU.not_equal, fill=1.0,
                                    base=0, pattern=[[-1, P]], channel_multiplier=1).then_inc(ident_ready, 1)
            nc.gpsimd.memset(ones[:, :].bitcast(F32), 1.0).then_inc(ones_ready, 1)
            pool.wait_ge(small_loaded, 64)
            nc.gpsimd.tensor_copy(row_hi[:, :], row_in[:, :]).then_inc(row_hi_ready, 1)
            pool.wait_ge(row_hi_ready, 1)
            nc.gpsimd.tensor_tensor(row_lo[:, :], row_in[:, :], row_hi[:, :].bitcast(F32),
                                    ALU.subtract).then_inc(row_lo_ready, 1)
            pool.wait_ge(w_loaded, 16)
            nc.gpsimd.tensor_copy(w_hi[:, :, :], w_in[:, :, :]).then_inc(w_hi_ready, 1)
            pool.wait_ge(w_hi_ready, 1)
            nc.gpsimd.tensor_tensor(w_lo[:, :, :], w_in[:, :, :], w_hi[:, :, :].bitcast(F32),
                                    ALU.subtract).then_inc(w_lo_ready, 1)
            pool.sem_inc(normed_free, 1)
            with pool.Fori(0, LAST) as m:
                pool.wait_ge(norm_ready, (m + 1) * TILES)
                pool.dma_start(out_chunks[:, bass.ds(m, 1), :], normed[:, :]).then_inc(stored, 16)
                pool.wait_ge(stored, (m + 1) * 16)
                pool.sem_inc(normed_free, 1)

        @block.tensor
        def _(pe):
            def accumulate(b, c, g):
                first = isinstance(c, int) and c == 0
                if first:
                    if b == 0 and g >= BY_SLOT:
                        pe.wait_ge(a_lo_ready, g + 1)
                    if g % XPG == 0:
                        pe.wait_ge(x_lo_ready, 2 * (g // XPG) + b + 1)
                else:
                    if b == 0 and g % 2 == 0:
                        pe.wait_ge(a_lo_ready, c * GROUPS + g + 2)
                    if g == 0:
                        pe.wait_ge(h_ready[b], (c - 1) * STAGES + 1)
                s = g % RING
                for u in range(GSLOTS):
                    t = g * GSLOTS + u
                    by_slot = first and b == 0 and g < BY_SLOT
                    if by_slot:
                        pe.wait_ge(a_hi_ready if u else first_hi_ready, g + 1)
                    xh = x_hi[:, b, t * D:(t + 1) * D]
                    xl = x_lo[:, b, t * D:(t + 1) * D]
                    ah = a_hi[:, s, u * COLS:(u + 1) * COLS]
                    al = a_lo[:, s, u * COLS:(u + 1) * COLS]
                    nc.tensor.matmul(acc[b][:, :], xh, ah, start=(t == 0), stop=False)
                    nc.tensor.matmul(acc[b][:, :], xl, ah, start=False, stop=False)
                    if by_slot:
                        pe.wait_ge(a_lo_ready if u else first_lo_ready, g + 1)
                    last = nc.tensor.matmul(acc[b][:, :], xh, al, start=False, stop=(t == T - 1))
                return last

            def weigh(bank, k, b, m, n, start, stop, half=None):
                split = half if b else None
                cols = columns(half)
                hh, hl, o = h_hi[:, b, cols], h_lo[:, b, cols], bank[:, cols]
                if split is None:
                    pe.wait_ge(h_lo_ready[b], count(m, STAGES, n, None))
                else:
                    pe.wait_ge(half_hi_ready, half_hi_count(n, half))
                nc.tensor.matmul(o, w_hi[:, k, :], hh, start=start, stop=False)
                nc.tensor.matmul(o, w_lo[:, k, :], hh, start=False, stop=False)
                if split is not None:
                    pe.wait_ge(h_lo_ready[b], count(m, STAGES, n, half))
                return nc.tensor.matmul(o, w_hi[:, k, :], hl, start=False, stop=stop)

            def layer(b, m, l, half=None):
                bank = mlp[b] if half is None else mlp2_half[l][half]
                weigh(bank, b * LAYERS + l, b, m, l, half is None, True, half).then_inc(layer_done[b], 1)

            def bias_first(l, half):
                bank = mlp2_half[l][half]
                for n, row in enumerate((row_hi, row_lo)):
                    nc.tensor.matmul(bank[:, columns(half)], row[:, l * D:(l + 1) * D], ones[:, :],
                                     start=(n == 0), stop=False)

            def merge(b, m):
                last = weigh(merged, 2 * LAYERS + b, b, m, LAYERS, b == 0, b == 1)
                if b == 1:
                    last.then_inc(merge_done, 1)

            def turn(m):
                pe.wait_ge(merged_ready, m + 1)
                for j in range(TILES):
                    last = nc.tensor.transpose(turned[:, j * P:(j + 1) * P], merged_sb[:, j * P:(j + 1) * P],
                                               ident[:, :])
                last.then_inc(rows_done, 1)

            def rows(half, j):
                return rows_half[half][:, j * P:(j + 1) * P]

            def rows_bias(half):
                for n, row in enumerate((row_hi, row_lo)):
                    nc.tensor.matmul(rows_half[half][:, columns(half)], ones[:, 0:P], row[:, LAYERS * D:],
                                     start=(n == 0), stop=False)

            def rows_high(b, half, j):
                hh = h_hi[:, b, j * P:(j + 1) * P]
                nc.tensor.matmul(rows(half, j), hh, w_hi[:, 2 * LAYERS + b, :], start=False, stop=False)
                nc.tensor.matmul(rows(half, j), hh, w_lo[:, 2 * LAYERS + b, :], start=False, stop=False)

            def rows_low(b, half, j, last=False):
                return nc.tensor.matmul(rows(half, j), h_lo[:, b, j * P:(j + 1) * P], w_hi[:, 2 * LAYERS + b, :],
                                        start=False, stop=last)

            def rows_branch1(half, j):
                pe.wait_ge(h_lo_ready[0], count(LAST, STAGES, LAYERS, None))
                rows_high(0, half, j)
                rows_low(0, half, j)

            def rows_branch2_high(half):
                pe.wait_ge(half_hi_ready, half_hi_count(LAYERS, half))
                for j in range(TILES)[tiles_of(half)]:
                    rows_high(1, half, j)

            def rows_branch2_low(half):
                pe.wait_ge(h_lo_ready[1], count(LAST, STAGES, LAYERS, half))
                for j in range(TILES)[tiles_of(half)]:
                    last = rows_low(1, half, j, j == tiles_of(half).stop - 1)
                last.then_inc(rows_done, 1)

            def mlp_step(m, s):
                if 2 <= s < 2 + 2 * LAYERS:
                    layer((s - 2) % 2, m, (s - 2) // 2)
                if s == 9:
                    merge(0, m)
                    merge(1, m)
                if s == 11:
                    turn(m)

            def chunk(c, m, lags, after=lambda left: None):
                behind = 0
                for s in range(GROUPS):
                    last = accumulate(0, c, s)
                    if s == GROUPS - 1:
                        last.then_inc(acc1_done, 1)
                    while behind <= s - lags[s]:
                        accumulate(1, c, behind).then_inc(group_used, 1)
                        behind += 1
                    if m is not None:
                        mlp_step(m, s)
                for g in range(behind, GROUPS):
                    accumulate(1, c, g).then_inc(group_used, 1)
                    after(GROUPS - 1 - g)

            def early_layers(left):
                if left in EARLY:
                    layer(0, LAST, EARLY.index(left))

            def keep_warm(bank, times):
                for _ in range(times):
                    nc.tensor.matmul(bank[:, :], zeros[:, 0:P], zeros[:, :], start=True, stop=True)

            pe.wait_ge(zeros_ready, 1)
            keep_warm(spare, WARM)
            chunk(0, None, FIRST_LAGS)
            pe.wait_ge(w_lo_ready, 1)
            pe.wait_ge(ident_ready, 1)
            pe.wait_ge(row_lo_ready, 1)
            pe.wait_ge(ones_ready, 1)
            with pe.Fori(1, LAST) as c:
                chunk(c, c - 1, LAGS)
            chunk(LAST, LAST - 1, LAST_LAGS, early_layers)
            for l in range(2):
                for half in range(2):
                    bias_first(l, half)
            for half in range(2):
                layer(1, LAST, 0, half)
            for half in range(2):
                bias_first(2, half)
            rows_bias(0)
            pe.wait_ge(h_ready[0], count(LAST, STAGES, LAYERS, None))
            rows_bias(1)
            for half in range(2):
                layer(1, LAST, 1, half)
            rows_branch1(0, 0)
            for half in range(2):
                layer(1, LAST, 2, half)
            rows_branch1(0, 1)
            rows_branch2_high(0)
            rows_branch2_low(0)
            rows_branch1(1, 2)
            rows_branch2_high(1)
            rows_branch1(1, 3)
            rows_branch2_low(1)

        @block.scalar
        def _(act):
            def x_high(j, b):
                act.wait_ge(x_loaded[b][j % 2], 16 * (j // 2 + 1))
                src = x1_sb[:, j * XCOLS:(j + 1) * XCOLS] if b == 0 else x2_in[:, j % 2, :]
                nc.scalar.copy(x_hi[:, b, j * XCOLS:(j + 1) * XCOLS], src).then_inc(x_hi_ready, 1)

            def a_high(c, g):
                s = g % RING
                if isinstance(c, int) and c == 0 and g < BY_SLOT:
                    for u, loaded, ready in ((0, first_loaded[g], first_hi_ready), (1, a_loaded[g], a_hi_ready)):
                        cols = slice(u * COLS, (u + 1) * COLS)
                        act.wait_ge(loaded, 16)
                        nc.scalar.copy(a_hi[:, s, cols], a_in[:, g, cols]).then_inc(ready, 1)
                    return
                act.wait_ge(a_loaded[g % LOADS], c * (16 * GROUPS // LOADS) + 16 * (g // LOADS + 1))
                if not (isinstance(c, int) and c == 0) or g >= RING:
                    act.wait_ge(group_used, c * GROUPS + (g - RING + 1))
                nc.scalar.copy(a_hi[:, s, :], a_in[:, g % LOADS, :]).then_inc(a_hi_ready, 1)

            def take_acc(b, m):
                if b == 0:
                    act.wait_ge(acc1_done, m + 1)
                else:
                    act.wait_ge(group_used, (m + 1) * GROUPS)
                dst, ready = (h_hi, half_hi_ready) if b == 1 and m is LAST else (h, h_ready[b])
                nc.scalar.activation(dst[:, b, :], acc[b][:, :], ACT.Copy,
                                     scale=gain[:, b:b + 1]).then_inc(ready, 1)

            def take_layer(b, m, l, half=None):
                act.wait_ge(layer_done[b], count(m, LAYERS, l, half))
                if half is None:
                    k = b * LAYERS + l
                    nc.scalar.activation(h[:, b, :], mlp[b][:, :], ACT.Relu,
                                         bias=bias_sb[:, k:k + 1]).then_inc(h_ready[b], 1)
                else:
                    cols = columns(half)
                    nc.scalar.activation(h_hi[:, b, cols], mlp2_half[l][half][:, cols],
                                         ACT.Relu).then_inc(half_hi_ready, 1)

            def take_merged(m):
                act.wait_ge(merge_done, m + 1)
                nc.scalar.activation(merged_sb[:, :], merged[:, :], ACT.Identity,
                                     bias=bm_sb[:, 0:1]).then_inc(merged_ready, 1)

            def deviation(m, half=None):
                tiles = tiles_of(half)
                act.wait_ge(var_ready, m * TILES + tiles.stop)
                nc.scalar.activation(std[:, tiles], mv[:, tiles, 1], ACT.Sqrt,
                                     bias=ln_eps[:, 0:1]).then_inc(std_ready, 1)

            def mlp_step(m, g):
                if g == 3:
                    take_acc(0, m)
                if g == 5:
                    take_acc(1, m)
                if 6 <= g < 6 + 2 * LAYERS:
                    take_layer((g - 6) % 2, m, (g - 6) // 2)
                if g == 12:
                    take_merged(m)
                if g == NORM_STEP + 2:
                    deviation(m)

            for g in range(GROUPS):
                if g == 0:
                    x_high(0, 0)
                a_high(0, g)
                if g > 0 and g % XPG == 0:
                    x_high(g // XPG, 0)
                if g % XPG == 0:
                    x_high(g // XPG, 1)
            act.wait_ge(ln_eps_ready, 1)
            act.wait_ge(gain_ready, 1)
            with act.Fori(1, LAST) as c:
                for g in range(GROUPS):
                    a_high(c, g)
                    mlp_step(c - 1, g)
            for g in range(GROUPS):
                a_high(LAST, g)
                if g < NORM_STEP:
                    mlp_step(LAST - 1, g)
            for b, n, half in TAIL:
                if (b, n) == (0, 2):
                    deviation(LAST - 1)
                if n == 0:
                    take_acc(b, LAST)
                else:
                    take_layer(b, LAST, n - 1, half)
            for half in range(2):
                deviation(LAST, half)

        @block.vector
        def _(dve):
            def x_low(j, b):
                dve.wait_ge(x_hi_ready, 2 * j + b + 1)
                cols = slice(j * XCOLS, (j + 1) * XCOLS)
                src = x1_sb[:, cols] if b == 0 else x2_in[:, j % 2, :]
                nc.vector.tensor_tensor(x_lo[:, b, cols], src, x_hi[:, b, cols].bitcast(F32),
                                        ALU.subtract).then_inc(x_lo_ready, 1)

            def a_low(c, g):
                s = g % RING
                if isinstance(c, int) and c == 0 and g < BY_SLOT:
                    for u, hi, ready in ((0, first_hi_ready, first_lo_ready), (1, a_hi_ready, a_lo_ready)):
                        cols = slice(u * COLS, (u + 1) * COLS)
                        dve.wait_ge(hi, g + 1)
                        nc.vector.tensor_tensor(a_lo[:, s, cols], a_in[:, g, cols], a_hi[:, s, cols].bitcast(F32),
                                                ALU.subtract).then_inc(ready, 1)
                    return
                dve.wait_ge(a_hi_ready, c * GROUPS + g + 1)
                nc.vector.tensor_tensor(a_lo[:, s, :], a_in[:, g % LOADS, :], a_hi[:, s, :].bitcast(F32),
                                        ALU.subtract).then_inc(a_lo_ready, 1)

            def high_h(b, m, n):
                dve.wait_ge(h_ready[b], count(m, STAGES, n, None))
                nc.vector.tensor_copy(h_hi[:, b, :], h[:, b, :]).then_inc(h_hi_ready[b], 1)

            def low_h(b, m, n):
                dve.wait_ge(h_hi_ready[b], count(m, STAGES, n, None))
                nc.vector.tensor_tensor(h_lo[:, b, :], h[:, b, :], h_hi[:, b, :].bitcast(F32),
                                        ALU.subtract).then_inc(h_lo_ready[b], 1)

            def split_h(b, m, n):
                high_h(b, m, n)
                low_h(b, m, n)

            def low_half(n, half):
                cols = columns(half)
                dve.wait_ge(half_hi_ready, half_hi_count(n, half))
                if n == 0:
                    bank, scalar, op = acc[1], gain[:, 1:2], ALU.mult
                else:
                    bank, scalar, op = mlp2_half[n - 1][half], 0.0, ALU.max
                nc.vector.scalar_tensor_tensor(out=h_lo[:, 1, cols], in0=bank[:, cols], scalar=scalar,
                                               in1=h_hi[:, 1, cols].bitcast(F32), op0=op,
                                               op1=ALU.subtract).then_inc(h_lo_ready[1], 1)

            def residual(m, half=None):
                cols = columns(half)
                dve.wait_ge(rows_done, count(m, 1, 0, half))
                bank = turned if half is None else rows_half[half]
                x = x1_sb[:, bass.ds(m * COLS + cols.start, cols.stop - cols.start)]
                nc.vector.tensor_tensor(y[:, cols], bank[:, cols], x, ALU.add).then_inc(y_ready, 1)

            def statistics(j):
                nc.vector.bn_stats(stats[:, j, :], y[:, j * D:(j + 1) * D]).then_inc(stats_ready, 1)

            def variance(j):
                nc.vector.bn_aggr(mv[:, j, :], stats[:, j, :]).then_inc(var_ready, 1)

            def invert(m, half=None):
                tiles = tiles_of(half)
                dve.wait_ge(std_ready, count(m, 1, 0, half))
                nc.vector.reciprocal(rstd[:, tiles], std[:, tiles]).then_inc(rstd_ready, 1)

            def refine(m, step, half=None):
                tiles = tiles_of(half)
                r = rstd[:, tiles]
                if step == 0:
                    dve.wait_ge(rstd_ready, count(m, 1, 0, half))
                    dst, src, add, times = var_rstd, mv[:, tiles, 1], EPS, None
                else:
                    dve.wait_ge(refined[step - 1], count(m, 1, 0, half))
                    if step == 1:
                        dst, src, add, times = half_square, var_rstd[:, tiles], None, -0.5
                    else:
                        dst, src, add, times = scale, half_square[:, tiles], 1.5, None
                nc.vector.scalar_tensor_tensor(out=dst[:, tiles], in0=src, scalar=times if add is None else add,
                                               in1=r, op0=ALU.mult if add is None else ALU.add,
                                               op1=ALU.mult).then_inc(refined[step], 1)

            def normalise(m, j, half=None):
                if j == tiles_of(half).start:
                    dve.wait_ge(refined[2], count(m, 1, 0, half))
                    if half != 1:
                        dve.wait_ge(normed_free, m + 1)
                nc.vector.tensor_scalar(normed[:, j * D:(j + 1) * D], y[:, j * D:(j + 1) * D],
                                        mv[:, j, 0:1], scale[:, j:j + 1], ALU.subtract,
                                        ALU.mult).then_inc(norm_ready, 1)

            def norm_step(m, step):
                if step == 0:
                    residual(m)
                    dve.wait_ge(y_ready, m + 1)
                    for j in range(TILES):
                        statistics(j)
                    dve.wait_ge(stats_ready, (m + 1) * TILES)
                elif step == 1:
                    for j in range(TILES):
                        variance(j)
                else:
                    invert(m)
                    for k in range(3):
                        refine(m, k)
                    for j in range(TILES):
                        normalise(m, j)

            def mlp_step(m, g):
                if g == 3:
                    split_h(0, m, 0)
                if g == 5:
                    split_h(1, m, 0)
                if 6 <= g < 6 + 2 * LAYERS:
                    split_h((g - 6) % 2, m, (g - 6) // 2 + 1)
                if g >= NORM_STEP:
                    norm_step(m, g - NORM_STEP)

            nc.vector.memset(zeros[:, :].bitcast(F32), 0.0).then_inc(zeros_ready, 1)
            for g in range(GROUPS):
                if g == 0:
                    x_low(0, 0)
                a_low(0, g)
                if g > 0 and g % XPG == 0:
                    x_low(g // XPG, 0)
                if g % XPG == 0:
                    x_low(g // XPG, 1)
                if g == 6:
                    dve.wait_ge(small_loaded, 64)
                    nc.vector.tensor_scalar(gain[:, :], eps_sb[:, :], 1.0, 1.0, ALU.add,
                                            ALU.add).then_inc(gain_ready, 1)
            with dve.Fori(1, LAST) as c:
                for g in range(GROUPS):
                    a_low(c, g)
                    mlp_step(c - 1, g)
            for g in range(GROUPS):
                a_low(LAST, g)
                if g < NORM_STEP:
                    mlp_step(LAST - 1, g)
            for b, n, half in TAIL:
                if (b, n) == (0, 1):
                    norm_step(LAST - 1, 0)
                    norm_step(LAST - 1, 1)
                if (b, n) == (0, 2):
                    norm_step(LAST - 1, 2)
                if (b, n) == (1, 0):
                    low_half(0, 0)
                    low_half(0, 1)
                elif (b, n) == (0, 3):
                    high_h(0, LAST, n)
                elif half is None:
                    split_h(b, LAST, n)
                else:
                    low_half(n, half)
                if (b, n, half) == (1, 1, 1):
                    low_h(0, LAST, 3)
            first, second = (range(TILES)[tiles_of(half)] for half in range(2))
            residual(LAST, 0)
            dve.wait_ge(y_ready, LAST + 1)
            for j in first:
                statistics(j)
            dve.wait_ge(stats_ready, LAST * TILES + first.stop)
            for j in first:
                variance(j)
            residual(LAST, 1)
            dve.wait_ge(y_ready, LAST + 2)
            for j in second:
                statistics(j)
            invert(LAST, 0)
            dve.wait_ge(stats_ready, LAST * TILES + second.stop)
            for j in second:
                variance(j)
            refine(LAST, 0, 0)
            refine(LAST, 1, 0)
            invert(LAST, 1)
            refine(LAST, 2, 0)
            for k, j in enumerate(first):
                refine(LAST, k, 1)
                normalise(LAST, j, 0)
            refine(LAST, 2, 1)
            for j in second:
                normalise(LAST, j, 1)


def kernel(x, adj, L0_gnn_x2, L0_gnn_eps1, L0_gnn_eps2, L0_gnn_W1, L0_gnn_b1, L0_gnn_W2, L0_gnn_b2,
           L0_gnn_Wm, L0_gnn_bm):
    import numpy as np
    import concourse.bacc as bacc
    from concourse.bass_utils import run_bass_kernel_spmd

    f = np.ascontiguousarray
    a = np.asarray(adj).reshape(P, CHUNKS, TILES, P, GROUPS, GSLOTS)
    a = f(a.transpose(1, 4, 3, 5, 2, 0)).reshape(CHUNKS, GROUPS, P, GCOLS)
    w1, w2, wm = np.asarray(L0_gnn_W1), np.asarray(L0_gnn_W2), np.asarray(L0_gnn_Wm)
    w = f(np.concatenate([w1, w2, wm.reshape(D, 2, D).transpose(1, 0, 2)]).transpose(2, 0, 1))
    b = f(np.concatenate([np.asarray(L0_gnn_b1), np.asarray(L0_gnn_b2)]).T)
    row = f(np.concatenate([np.asarray(L0_gnn_b2)] + [np.asarray(L0_gnn_bm).reshape(1, D)] * (HALF // D)))
    row = row.reshape(1, ROW)
    e = np.concatenate([np.asarray(L0_gnn_eps1), np.asarray(L0_gnn_eps2)]).reshape(1, 2)
    arrays = {"x1": f(x), "x2": f(L0_gnn_x2), "adj_t": a, "wts": w, "bias": b,
              "eps": f(e), "bias_row": row,
              "bm": f(L0_gnn_bm).reshape(D, 1)}

    nc = bacc.Bacc("TRN2", target_bir_lowering=False, num_devices=1)
    ins = [nc.dram_tensor(k, v.shape, mybir.dt.from_np(v.dtype), kind="ExternalInput").ap()
           for k, v in arrays.items()]
    out = nc.dram_tensor("out", (N, D), F32, kind="ExternalOutput").ap()
    build(nc, *ins, out)
    r = run_bass_kernel_spmd(nc, [arrays], core_ids=[0])
    return r.results[0]["out"]
```
